# Optimizing a Trainium2 kernel written in Bass

```python
import numpy as np
import jax
import jax.numpy as jnp

def _softmax(x, axis=-1):
    return jax.nn.softmax(x, axis=axis)
def _gelu(x):
    return jax.nn.gelu(x, approximate=True)
def _silu(x):
    return jax.nn.silu(x)
def _sigmoid(x):
    return jax.nn.sigmoid(x)
def _layernorm(x, axis=-1, eps=1e-5):
    m = jnp.mean(x, axis=axis, keepdims=True)
    v = jnp.var(x, axis=axis, keepdims=True)
    return (x - m) / jnp.sqrt(v + eps)
def _scatter_add(tgt, idx, src, axis=0):
    return tgt.at[idx].add(src)
def _segment_sum(src, seg, n):
    return jax.ops.segment_sum(src, seg, n)

kernel_name = 'mk_conv_seq_d1_conv_nchw512_04324b'

def setup_inputs(seed: int = 0):
    np.random.seed(seed)
    _w = jnp.asarray
    def _rec_inputs():
        import jax
        import jax.numpy as jnp
        _gk = jax.random.key(seed)
        x = 7.22e-05 + 1 * jax.random.normal(jax.random.fold_in(_gk, 1), (16, 512, 32, 32), jnp.float32)
        return x
    x = _rec_inputs()
    def _L0_conv_setup():
        import jax, jax.numpy as jnp
        import numpy as np
        B, C, H, W = (16, 512, 32, 32)
        G = 8
        EPS = 1e-05
        key = jax.random.key(seed)
        ks = jax.random.split(key, 6)
        s = 1.0 / np.sqrt(C)
        return {'x': jax.random.normal(ks[0], (B, C, H, W), jnp.float32), 'gamma': jnp.ones((C,), jnp.float32), 'beta': jnp.zeros((C,), jnp.float32), 'wq': jax.random.normal(ks[1], (C, C), jnp.float32) * s, 'bq': jnp.zeros((C,), jnp.float32), 'wk': jax.random.normal(ks[2], (C, C), jnp.float32) * s, 'bk': jnp.zeros((C,), jnp.float32), 'wv': jax.random.normal(ks[3], (C, C), jnp.float32) * s, 'bv': jnp.zeros((C,), jnp.float32), 'wp': jax.random.normal(ks[4], (C, C), jnp.float32) * s, 'bp': jnp.zeros((C,), jnp.float32)}
    _L0_conv_all = _L0_conv_setup()
    _L0_conv_in = {k: v for k, v in _L0_conv_all.items() if k in ('gamma', 'beta', 'wq', 'bq', 'wk', 'bk', 'wv', 'bv', 'wp', 'bp', )}
    del _L0_conv_all

    return {
        "x": x,
        "L0_conv_gamma": _L0_conv_in["gamma"],
        "L0_conv_beta": _L0_conv_in["beta"],
        "L0_conv_wq": _L0_conv_in["wq"],
        "L0_conv_bq": _L0_conv_in["bq"],
        "L0_conv_wk": _L0_conv_in["wk"],
        "L0_conv_bk": _L0_conv_in["bk"],
        "L0_conv_wv": _L0_conv_in["wv"],
        "L0_conv_bv": _L0_conv_in["bv"],
        "L0_conv_wp": _L0_conv_in["wp"],
        "L0_conv_bp": _L0_conv_in["bp"],
    }

def reference(x, L0_conv_gamma, L0_conv_beta, L0_conv_wq, L0_conv_bq, L0_conv_wk, L0_conv_bk, L0_conv_wv, L0_conv_bv, L0_conv_wp, L0_conv_bp):
    import jax
    import jax.numpy as jnp
    def _L0_conv_ref(x, gamma, beta, wq, bq, wk, bk, wv, bv, wp, bp):
        import jax, jax.numpy as jnp
        import numpy as np
        B, C, H, W = (16, 512, 32, 32)
        G = 8
        EPS = 1e-05
        b, c, h, w = x.shape
        n = h * w
        xg = x.reshape(b, G, c // G, n)
        mean = xg.mean(axis=(2, 3), keepdims=True)
        var = xg.var(axis=(2, 3), keepdims=True)
        xn = ((xg - mean) * jax.lax.rsqrt(var + EPS)).reshape(b, c, n)
        xn = xn * gamma[:, None] + beta[:, None]
        q = jnp.einsum('oc,bcn->bon', wq, xn) + bq[:, None]
        k = jnp.einsum('oc,bcn->bon', wk, xn) + bk[:, None]
        v = jnp.einsum('oc,bcn->bon', wv, xn) + bv[:, None]
        scale = 1.0 / c ** 0.5
        attn = jax.nn.softmax(jnp.einsum('bci,bcj->bij', q, k) * scale, axis=-1)
        out = jnp.einsum('bcj,bij->bci', v, attn)
        out = jnp.einsum('oc,bcn->bon', wp, out) + bp[:, None]
        return x + out.reshape(b, c, h, w)

    def _gn(v, G=32, eps=1e-5):
        B_, C_, H_, W_ = v.shape
        g = v.reshape(B_, G, C_ // G, H_, W_)
        m = jnp.mean(g, axis=(2, 3, 4), keepdims=True)
        s = jnp.var(g, axis=(2, 3, 4), keepdims=True)
        return ((g - m) / jnp.sqrt(s + eps)).reshape(v.shape)

    def _ln_c(v, eps=1e-6):
        m = jnp.mean(v, axis=1, keepdims=True)
        s = jnp.var(v, axis=1, keepdims=True)
        return (v - m) / jnp.sqrt(s + eps)

    def _ln_t(v, eps=1e-5):
        m = jnp.mean(v, axis=-1, keepdims=True)
        s = jnp.var(v, axis=-1, keepdims=True)
        return (v - m) / jnp.sqrt(s + eps)

    def _to_tokens(v):
        B_, C_, H_, W_ = v.shape
        return v.reshape(B_, C_, H_ * W_).transpose(0, 2, 1)
    def _from_tokens(t, like):
        B_, C_, H_, W_ = like.shape
        return t.transpose(0, 2, 1).reshape(B_, C_, H_, W_)

    x = _L0_conv_ref(x, L0_conv_gamma, L0_conv_beta, L0_conv_wq, L0_conv_bq, L0_conv_wk, L0_conv_bk, L0_conv_wv, L0_conv_bv, L0_conv_wp, L0_conv_bp)
    return x


_drawn_inputs = setup_inputs


def setup_inputs(seed=0):
    import zlib

    import numpy as np

    out = dict(_drawn_inputs(seed))
    spreads = {'L0_conv_gamma': (1.0, 0.2),
     'L0_conv_beta': (0.0, 0.1),
     'L0_conv_bq': (0.0, 0.8),
     'L0_conv_bk': (0.0, 0.8),
     'L0_conv_bv': (0.0, 0.1),
     'L0_conv_bp': (0.0, 0.1)}
    factors = {}
    for name, (base, spread) in spreads.items():
        noise = np.random.default_rng([zlib.crc32(name.encode()), seed]).standard_normal(out[name].shape)
        drawn = base * np.exp(spread * noise) if base else spread * noise
        out[name] = jnp.asarray(drawn.astype(out[name].dtype))
    for name, factor in factors.items():
        out[name] = (out[name] * factor).astype(out[name].dtype)
    return out
```

```python
from contextlib import ExitStack

import concourse.bass as bass
from concourse import mybir


def groupnorm_attention(nc, x, wq, wk, wv, wp_t, vectors, out):
    f32 = mybir.dt.float32
    f32r = mybir.dt.float32r
    ALU = mybir.AluOpType
    ACT = mybir.ActivationFunctionType

    P = 128
    B, C, N = x.shape
    GROUPS = 8
    EPS = 1e-5
    CT = C // P
    NT = N // P
    H = 512
    NH = N // H
    GC = C // GROUPS
    SCALE = float(C) ** -0.5
    JT = H // P
    assert NH == 2 and C == H and P % GC == 0

    SETUP_JOBS = 4
    JOBS = CT + NT + NT // 2 + CT
    Y0, S0 = 0, CT
    Z0 = S0 + NT
    V0 = Z0 + NT // 2
    assert JOBS % 2 == 0 and SETUP_JOBS % 2 == 0
    SETUP_SIDE = 4
    SIDE_T = 1
    SIDE_STAT = SIDE_T + 2 * NT
    SIDES = SIDE_STAT + 2

    ctx = ExitStack()
    with ctx:
        def sb(name, shape, dt=f32):
            return ctx.enter_context(nc.sbuf_tensor(name, shape, dt))

        def sem(name):
            return ctx.enter_context(nc.semaphore(name))

        x_in = sb("x_in", [P, CT, N])
        x_res = sb("x_res", [P, 2, N])
        xn_hi, xn_lo = sb("xn_hi", [P, CT, N], f32r), sb("xn_lo", [P, CT, N], f32r)
        yz_hi, yz_lo = sb("yz_hi", [P, CT * N], f32r), sb("yz_lo", [P, CT * N], f32r)
        at_hi, at_lo = sb("at_hi", [P, NT, N], f32r), sb("at_lo", [P, NT, N], f32r)
        m_hi, m_lo = sb("m_hi", [P, CT, C], f32r), sb("m_lo", [P, CT, C], f32r)
        n_hi, n_lo = sb("n_hi", [P, CT, C], f32r), sb("n_lo", [P, CT, C], f32r)
        work = sb("work", [P, 4, N])
        r_part = sb("r_part", [P, N])
        ident = sb("ident", [P, P])
        group_mean = sb("group_mean", [P, P])
        ones = sb("ones", [P, P])
        ones_r = sb("ones_r", [P, P], f32r)
        vec = sb("vec", [P, 6, CT])
        gamma, beta, bq, bk, bv, bp = (vec[:, n, :] for n in range(6))
        wu = sb("wu", [P, 2 * CT + 1])
        w_col, u_col, r_const = wu[:, 0:CT], wu[:, CT:2 * CT], wu[:, 2 * CT:2 * CT + 1]
        g_col = sb("g_col", [P, CT])
        bqk = sb("bqk", [P, CT])
        stats = sb("stats", [P, CT, NH, 6])
        mean_var = sb("mean_var", [P, CT, 2])
        mean_g, dev, sq, sqv, var_g = (sb(n, [P, CT]) for n in ("mean_g", "dev", "sq", "sqv", "var_g"))
        half_neg, rstd, x_scale, ms, x_shift = (
            sb(n, [P, CT]) for n in ("half_neg", "rstd", "x_scale", "ms", "x_shift"))
        neg_max, row_sum, row_inv = (sb(n, [P, NT]) for n in ("neg_max", "row_sum", "row_inv"))

        y_hi, y_lo = (t[:, :].rearrange("p (c n) -> p c n", c=CT) for t in (yz_hi, yz_lo))
        z_hi, z_lo = (t[:, :].rearrange("p (t c) -> p t c", t=NT) for t in (yz_hi, yz_lo))
        PB = 3
        prob = [work[:, n, :] for n in range(PB)]
        r_row = work[:, PB, :]
        wk_in, wq_in = (work[:, 2 * n:2 * n + 2, :].rearrange("p a (b c) -> p (a b) c", c=C) for n in range(2))
        wv_in = x_res[:, :, :].rearrange("p a (b c) -> p (a b) c", c=C)
        wp_in = wk_in
        parts_hi, parts_lo = (
            [t[:, 2 * n:2 * n + 2, :].rearrange("p a (b c) -> p (a b) c", c=C) for n in range(4)]
            for t in (at_hi, at_lo))
        WK, WQ, WV, WP = range(4)

        acc = [ctx.enter_context(nc.psum_tensor(f"acc{n}", [P, N], f32)) for n in range(2)]
        side = ctx.enter_context(nc.psum_tensor("side", [P, NH, H], f32))

        vec_loaded = sem("vec_loaded")
        w_loaded = [sem(f"w{n}_loaded") for n in range(4)]
        x_loaded = [sem(f"x_loaded{n}") for n in range(CT)]
        res_loaded = [sem(f"res_loaded{n}") for n in range(2)]
        out_stored = [sem(f"out_stored{n}") for n in range(2)]
        consts_ready = sem("consts_ready")
        ident_zeroed = sem("ident_zeroed")
        setup_ready = sem("setup_ready")
        w_hi_ready, w_lo_ready = sem("w_hi_ready"), sem("w_lo_ready")
        acc_filled, acc_hi_ready, acc_drained = sem("acc_filled"), sem("acc_hi_ready"), sem("acc_drained")
        side_filled, side_hi_ready, side_drained = sem("side_filled"), sem("side_hi_ready"), sem("side_drained")
        exp_ready, inv_ready, prob_ready = sem("exp_ready"), sem("inv_ready"), sem("prob_ready")
        stats_ready, mean_ready = sem("stats_ready"), sem("mean_ready")
        norm_step, rstd_ready = sem("norm_step"), sem("rstd_ready")
        xn_ready, xn_hi_ready, xn_lo_ready = sem("xn_ready"), sem("xn_hi_ready"), sem("xn_lo_ready")
        x_used = sem("x_used")
        r_hi_ready, r_lo_ready = sem("r_hi_ready"), sem("r_lo_ready")
        gates = sem("gates")
        NORM_STEPS = 6

        block = ctx.enter_context(nc.Block())

        def images(eng, image):
            with eng.Fori(0, B - 1) as b:
                image(b, True)
            image(B - 1, False)

        @block.sync
        def _(sp):
            weight = lambda w: w.rearrange("(t p) c -> p t c", p=P)
            sp.dma_start(wk_in, weight(wk)).then_inc(w_loaded[WK], 16)
            sp.dma_start(wq_in, weight(wq)).then_inc(w_loaded[WQ], 16)
            sp.dma_start(vec[:, :, :], vectors.rearrange("p (n c) -> p n c", n=6)).then_inc(vec_loaded, 16)
            sp.dma_start(wv_in, weight(wv)).then_inc(w_loaded[WV], 16)

            def load_x(b):
                for c in range(CT):
                    sp.dma_start(x_in[:, c, :], x[b, c * P:(c + 1) * P, :]).then_inc(x_loaded[c], 16)

            load_x(0)
            sp.wait_ge(w_lo_ready, WK + 1)
            sp.wait_ge(side_filled, 1)
            sp.dma_start(wp_in, weight(wp_t)).then_inc(w_loaded[WP], 16)
            sp.wait_ge(w_lo_ready, WV + 1)

            def load_res(b, c):
                sp.dma_start(x_res[:, c % 2, :], x[b, c * P:(c + 1) * P, :]).then_inc(res_loaded[c % 2], 16)

            def image(b, more):
                if more:
                    sp.wait_ge(x_used, CT * b + CT)
                    load_x(b + 1)
                for c in range(CT):
                    sp.wait_ge(acc_drained, SETUP_JOBS + JOBS * b + V0 + c + 1)
                    sp.dma_start(out[b, c * P:(c + 1) * P, :], x_res[:, c % 2, :]).then_inc(out_stored[c % 2], 16)
                    if c + 2 < CT:
                        sp.wait_ge(out_stored[c % 2], 16 * (CT // 2) * b + 16 * (c // 2 + 1))
                        load_res(b, c + 2)

                for c in range(2):
                    sp.wait_ge(out_stored[c], 16 * (CT // 2) * b + 16 * (CT // 2))
                    if more:
                        load_res(b + 1, c)

            for c in range(2):
                load_res(0, c)
            images(sp, image)

        @block.gpsimd
        def _(pool):
            pool.memset(ident[:, :], 0.0).then_inc(ident_zeroed, 1)
            pool.memset(ones[:, :], 1.0).then_inc(consts_ready, 1)
            pool.memset(half_neg[:, :], -0.5).then_inc(ident_zeroed, 1)
            pool.wait_ge(ident_zeroed, 1)
            pool.affine_select(out=ident[:, :], in_=ident[:, :], compare_op=ALU.not_equal, fill=1.0,
                               base=0, pattern=[[-1, P]], channel_multiplier=1).then_inc(consts_ready, 1)
            pool.wait_ge(ident_zeroed, 2)

            def rsqrt(n, var_drained):
                pool.wait_ge(side_drained, var_drained)
                pool.tensor_tensor(rstd[:, :], var_g[:, :], half_neg[:, :], ALU.pow).then_inc(rstd_ready, 1)

            rsqrt(0, SETUP_SIDE)
            with pool.Fori(0, B - 1) as b:
                rsqrt(b + 1, SETUP_SIDE + SIDES * b + SIDES)

        @block.tensor
        def _(pe):
            def claim(job):
                if not isinstance(job, int) or job >= 2:
                    pe.wait_ge(acc_drained, job - 1)

            def passes(k_hi, k_lo, streams):
                return ([(k_hi, s, 0) for s in range(streams)] + [(k_hi, s, 1) for s in range(streams)]
                        + [(k_lo, s, 0) for s in range(streams)])

            def rows_job(job, slot, l_hi, l_lo, r_hi, r_lo, before=None, between=None):
                claim(job)
                K = len(l_hi)
                for k in range(K):
                    if before is not None:
                        before(k)
                    for n, (l, h, part) in enumerate(passes(l_hi[k], l_lo[k], NH)):
                        r = (r_hi, r_lo)[part][k]
                        last = pe.matmul(acc[slot][:, h * H:(h + 1) * H], l, r[:, h * H:(h + 1) * H],
                                         start=(k == 0 and n < NH), stop=(k == K - 1 and n >= 2 * NH))
                    if k == K - 1:
                        last.then_inc(acc_filled, 1)
                    if between is not None:
                        between(k)

            def tiles_job(job, slot, tiles, l_hi, l_lo, r_hi, r_lo, between=None):
                claim(job)
                for n, t in enumerate(tiles):
                    for k in range(CT):
                        cols = slice(t * P, (t + 1) * P)
                        for m, (l, _, part) in enumerate(passes(l_hi[:, k, cols], l_lo[:, k, cols], 1)):
                            last = pe.matmul(acc[slot][:, n * H:(n + 1) * H], l, (r_hi, r_lo)[part][:, k, :],
                                             start=(k == 0 and m == 0), stop=(k == CT - 1 and m == 2))
                    if n == len(tiles) - 1:
                        last.then_inc(acc_filled, 1)
                    if between is not None:
                        between(n)

            def group_sum(bank, job, values):
                pe.wait_ge(side_drained, job - 1)
                pe.matmul(side[:, bank, 0:CT], group_mean[:, :], values, start=True, stop=True).then_inc(side_filled, 1)

            def group_sum_mean(nb, job):
                pe.wait_ge(mean_ready, CT * nb + CT)
                group_sum(0, job, mean_var[:, :, 0])

            def group_sum_var(nb, job):
                pe.wait_ge(norm_step, NORM_STEPS * nb + 3)
                group_sum(1, job, sqv[:, :])

            pe.wait_ge(consts_ready, 2)
            pe.wait_ge(vec_loaded, 16)
            pe.wait_ge(w_loaded[WK], 16)
            pe.wait_ge(w_loaded[WQ], 16)
            for n, (w, v) in enumerate(((wk_in, bq), (wq_in, bk))):
                for c in range(CT):
                    for k in range(CT):
                        pe.matmul(side[:, 0, n * CT + c:n * CT + c + 1], w[:, k, c * P:(c + 1) * P], v[:, k:k + 1],
                                  start=(k == 0), stop=(k == CT - 1))
            pe.wait_ge(setup_ready, P // GC + 3)
            for k in range(CT):
                last = pe.matmul(side[:, 0, 2 * CT:2 * CT + 1], ones[:, :], bqk[:, k:k + 1],
                                 start=(k == 0), stop=(k == CT - 1))
            last.then_inc(side_filled, 1)
            pe.wait_ge(w_lo_ready, WQ + 1)
            for n in range(2):
                tiles_job(n, n % 2, (2 * n, 2 * n + 1), parts_hi[WK], parts_lo[WK], parts_hi[WQ], parts_lo[WQ])
            pe.wait_ge(w_loaded[WP], 16)
            for c in range(CT):
                for k in range(CT):
                    last = pe.matmul(side[:, 1, c:c + 1], wp_in[:, k, c * P:(c + 1) * P], bv[:, k:k + 1],
                                     start=(k == 0), stop=(k == CT - 1))
            last.then_inc(side_filled, 1)
            group_sum_mean(0, 2)
            pe.wait_ge(w_lo_ready, WP + 1)
            tiles_job(2, 0, (0, 1), parts_hi[WV], parts_lo[WV], parts_hi[WP], parts_lo[WP])
            group_sum_var(0, 3)
            tiles_job(3, 1, (2, 3), parts_hi[WV], parts_lo[WV], parts_hi[WP], parts_lo[WP])

            def image(b, more):
                job = SETUP_JOBS + JOBS * b
                sjob = SETUP_SIDE + SIDES * b

                def transposes(i, h):
                    n = SIDE_T + 2 * i + h
                    if h == 0:
                        pe.wait_ge(prob_ready, NT * b + i + 1)
                    pe.wait_ge(side_drained, sjob + (1 if i == 0 else n - 1))
                    for t in range(JT):
                        j = h * JT + t
                        last = pe.transpose(side[:, h, t * P:(t + 1) * P], prob[i % PB][:, j * P:(j + 1) * P], ident[:, :])
                    last.then_inc(side_filled, 1)

                for c in range(CT):
                    cols = slice(c * P, (c + 1) * P)

                    def chunk_ready(k):
                        pe.wait_ge(xn_lo_ready, CT * b + k + 1)
                    rows_job(job + Y0 + c, c % 2, [m_hi[:, k, cols] for k in range(CT)],
                             [m_lo[:, k, cols] for k in range(CT)],
                             [xn_hi[:, k, :] for k in range(CT)], [xn_lo[:, k, :] for k in range(CT)],
                             before=chunk_ready if c == 0 else None)
                    if c == 1:
                        pe.wait_ge(r_lo_ready, b + 1)
                        pe.wait_ge(side_drained, sjob)
                        for h in range(NH):
                            for m, part in enumerate((at_hi, at_lo)):
                                last = pe.matmul(side[:, h, :], ones_r[:, :], part[:, 0, h * H:(h + 1) * H],
                                                 start=(m == 0), stop=(m == 1))
                        last.then_inc(side_filled, 1)

                for i in range(NT):
                    cols = slice(i * P, (i + 1) * P)

                    def y_ready(k):
                        pe.wait_ge(acc_drained, job + Y0 + k + 1)

                    def turn(k):
                        if i >= 2 and k % 2 == 1:
                            transposes(i - 2, k // 2)
                    rows_job(job + S0 + i, i % 2, [xn_hi[:, k, cols] for k in range(CT)],
                             [xn_lo[:, k, cols] for k in range(CT)],
                             [y_hi[:, k, :] for k in range(CT)], [y_lo[:, k, :] for k in range(CT)],
                             before=y_ready if i == 0 else None, between=turn)

                for z in range(NT // 2):
                    def turn(n):
                        if z < 2:
                            transposes(NT - 2 + z, n)
                    tiles_job(job + Z0 + z, z % 2, (2 * z, 2 * z + 1), xn_hi, xn_lo, n_hi, n_lo, between=turn)

                for c in range(CT):
                    cols = slice(c * P, (c + 1) * P)

                    def z_ready(k):
                        if k == 0:
                            pe.wait_ge(side_drained, sjob + SIDE_STAT)
                        if k % 2 == 0:
                            pe.wait_ge(acc_drained, job + Z0 + k // 2 + 1)

                    def sums(k):
                        if more and k == 5 and c == 0:
                            group_sum_mean(b + 1, sjob + SIDE_STAT)
                        if more and k == 5 and c == 1:
                            group_sum_var(b + 1, sjob + SIDE_STAT + 1)
                    rows_job(job + V0 + c, c % 2, [z_hi[:, k, cols] for k in range(NT)],
                             [z_lo[:, k, cols] for k in range(NT)],
                             [at_hi[:, k, :] for k in range(NT)], [at_lo[:, k, :] for k in range(NT)],
                             before=z_ready if c == 0 else None, between=sums)

            images(pe, image)

        @block.scalar
        def _(act):
            def split_weight(n, dst, src):
                act.wait_ge(w_loaded[n], 16)
                act.activation(dst, src, ACT.Copy).then_inc(w_hi_ready, 1)

            def acc_hi(job, slot, dst, bias=None):
                act.wait_ge(acc_filled, job + 1)
                if bias is None:
                    ins = act.activation(dst, acc[slot][:, :], ACT.Copy)
                else:
                    ins = act.activation(dst, acc[slot][:, :], ACT.Identity, bias=bias)
                ins.then_inc(acc_hi_ready, 1)

            def normalise(nb):
                for c in range(CT):
                    act.wait_ge(xn_ready, CT * nb + c + 1)
                    if c == 0 and not (isinstance(nb, int) and nb == 0):
                        act.wait_ge(acc_filled, SETUP_JOBS + JOBS * nb - JOBS + V0)
                    act.activation(xn_hi[:, c, :], x_in[:, c, :], ACT.Copy).then_inc(xn_hi_ready, 1)

            def split_r(nb):
                act.wait_ge(x_used, CT * nb + CT)
                act.wait_ge(acc_filled, SETUP_JOBS + JOBS * nb)
                act.activation(at_hi[:, 0, :], r_part[:, :], ACT.Copy).then_inc(r_hi_ready, 1)

            split_weight(WK, parts_hi[WK], wk_in)
            split_weight(WQ, parts_hi[WQ], wq_in)
            for n in range(2):
                acc_hi(n, n % 2, m_hi[:, 2 * n:2 * n + 2, :].rearrange("p a c -> p (a c)"))
            split_weight(WV, parts_hi[WV], wv_in)
            split_weight(WP, parts_hi[WP], wp_in)
            acc_hi(2, 0, n_hi[:, 0:2, :].rearrange("p a c -> p (a c)"))
            acc_hi(3, 1, n_hi[:, 2:4, :].rearrange("p a c -> p (a c)"))
            normalise(0)
            split_r(0)

            def image(b, more):
                job = SETUP_JOBS + JOBS * b
                sjob = SETUP_SIDE + SIDES * b

                def turned_hi(i, h):
                    act.wait_ge(side_filled, sjob + SIDE_T + 2 * i + h + 1)
                    act.activation(at_hi[:, h * JT:(h + 1) * JT, i * P:(i + 1) * P],
                                   side[:, h, :].rearrange("p (t n) -> p t n", t=JT), ACT.Copy).then_inc(side_hi_ready, 1)

                for c in range(CT):
                    acc_hi(job + Y0 + c, c % 2, y_hi[:, c, :], bias=u_col[:, c:c + 1])
                for n in range(NT + NT // 2):
                    if 2 <= n < NT + 2:
                        turned_hi(n - 2, 0)
                        turned_hi(n - 2, 1)
                    if n < NT:
                        act.wait_ge(acc_drained, job + S0 + n + 1)
                        act.activation(prob[n % PB], prob[n % PB], ACT.Exp, bias=neg_max[:, n:n + 1], scale=-1.0,
                                       accum_out=row_sum[:, n:n + 1]).then_inc(exp_ready, 1)
                    else:
                        z = n - NT
                        acc_hi(job + Z0 + z, z % 2, yz_hi[:, 2 * z * C:(2 * z + 2) * C])
                if more:
                    normalise(b + 1)
                    split_r(b + 1)

            images(act, image)

        @block.vector
        def _(dve):
            def split_weight(n, hi, lo, src):
                dve.wait_ge(w_hi_ready, n + 1)
                dve.tensor_tensor(lo, src, hi.bitcast(f32), ALU.subtract).then_inc(w_lo_ready, 1)

            SETUP_HI, HIS = SETUP_JOBS, CT + NT // 2

            def acc_lo(his, slot, lo, hi):
                dve.wait_ge(acc_hi_ready, his)
                dve.tensor_tensor(lo, acc[slot][:, :], hi.bitcast(f32), ALU.subtract).then_inc(acc_drained, 1)

            def gate(semaphore, value):
                dve.wait_ge(semaphore, value)
                dve.sem_inc(gates, 1)

            def channel_stats(nb, c):
                dve.wait_ge(x_loaded[c], 16 * nb + 16)
                for h in range(NH):
                    dve.bn_stats(stats[:, c, h, :], x_in[:, c, h * H:(h + 1) * H]).then_inc(stats_ready, 1)
                gate(stats_ready, NH * (CT * nb + c + 1))
                dve.bn_aggr(mean_var[:, c, :], stats[:, c, :, :].rearrange("p h s -> p (h s)")).then_inc(mean_ready, 1)

            def group_mean_in(nb, filled):
                dve.wait_ge(side_filled, filled)
                dve.wait_ge(mean_ready, CT * nb + CT)
                dve.tensor_copy(mean_g[:, :], side[:, 0, 0:CT]).then_inc(norm_step, 1)
                dve.tensor_tensor(dev[:, :], mean_var[:, :, 0], side[:, 0, 0:CT], ALU.subtract).then_inc(side_drained, 1)
                dve.wait_ge(side_drained, filled)
                dve.tensor_tensor(sq[:, :], dev[:, :], dev[:, :], ALU.mult).then_inc(norm_step, 1)
                dve.wait_ge(norm_step, NORM_STEPS * nb + 2)
                dve.tensor_tensor(sqv[:, :], sq[:, :], mean_var[:, :, 1], ALU.add).then_inc(norm_step, 1)

            def group_var_in(nb, filled):
                dve.wait_ge(side_filled, filled)
                dve.tensor_scalar(var_g[:, :], side[:, 1, 0:CT], EPS, None, ALU.add).then_inc(side_drained, 1)
                dve.wait_ge(rstd_ready, nb + 1)
                dve.tensor_tensor(x_scale[:, :], rstd[:, :], gamma, ALU.mult).then_inc(norm_step, 1)
                dve.wait_ge(norm_step, NORM_STEPS * nb + 4)
                dve.tensor_tensor(ms[:, :], mean_g[:, :], x_scale[:, :], ALU.mult).then_inc(norm_step, 1)
                dve.wait_ge(norm_step, NORM_STEPS * nb + 5)
                dve.tensor_tensor(x_shift[:, :], beta, ms[:, :], ALU.subtract).then_inc(norm_step, 1)
                dve.wait_ge(norm_step, NORM_STEPS * nb + 6)

            def normalise(c):
                dve.tensor_scalar(x_in[:, c, :], x_in[:, c, :], x_scale[:, c:c + 1], x_shift[:, c:c + 1],
                                  ALU.mult, ALU.add).then_inc(xn_ready, 1)

            def split_xn(nb, c):
                dve.wait_ge(xn_hi_ready, CT * nb + c + 1)
                dve.tensor_tensor(xn_lo[:, c, :], x_in[:, c, :], xn_hi[:, c, :].bitcast(f32),
                                  ALU.subtract).then_inc(xn_lo_ready, 1)

            def add_r(nb, c):
                if c == 0:
                    dve.tensor_scalar(r_part[:, :], x_in[:, c, :], w_col[:, c:c + 1], None, ALU.mult).then_inc(x_used, 1)
                else:
                    dve.wait_ge(x_used, CT * nb + c)
                    dve.scalar_tensor_tensor(r_part[:, :], x_in[:, c, :], w_col[:, c:c + 1], r_part[:, :],
                                             ALU.mult, ALU.add).then_inc(x_used, 1)

            def split_r(nb):
                dve.wait_ge(r_hi_ready, nb + 1)
                dve.tensor_tensor(at_lo[:, 0, :], r_part[:, :], at_hi[:, 0, :].bitcast(f32),
                                  ALU.subtract).then_inc(r_lo_ready, 1)

            dve.memset(group_mean[:, :], 0.0).then_inc(setup_ready, 1)
            dve.wait_ge(setup_ready, 1)
            for g in range(P // GC):
                rows = slice(g * GC, (g + 1) * GC)
                dve.memset(group_mean[rows, rows], 1.0 / GC).then_inc(setup_ready, 1)
            dve.wait_ge(vec_loaded, 16)
            dve.tensor_tensor(bqk[:, :], bq, bk, ALU.mult).then_inc(setup_ready, 1)
            dve.wait_ge(consts_ready, 1)
            dve.tensor_copy(ones_r[:, :], ones[:, :]).then_inc(setup_ready, 1)
            split_weight(WK, parts_hi[WK], parts_lo[WK], wk_in)
            split_weight(WQ, parts_hi[WQ], parts_lo[WQ], wq_in)
            dve.wait_ge(side_filled, 1)
            dve.tensor_copy(wu[:, :], side[:, 0, 0:2 * CT + 1]).then_inc(side_drained, 1)
            for n in range(2):
                rows = slice(2 * n, 2 * n + 2)
                acc_lo(n + 1, n % 2, m_lo[:, rows, :].rearrange("p a c -> p (a c)"),
                       m_hi[:, rows, :].rearrange("p a c -> p (a c)"))
            split_weight(WV, parts_hi[WV], parts_lo[WV], wv_in)
            for c in range(CT):
                channel_stats(0, c)
            split_weight(WP, parts_hi[WP], parts_lo[WP], wp_in)
            dve.wait_ge(side_filled, 2)
            dve.tensor_tensor(g_col[:, :], side[:, 1, 0:CT], bp, ALU.add).then_inc(side_drained, 1)
            group_mean_in(0, 3)
            acc_lo(3, 0, n_lo[:, 0:2, :].rearrange("p a c -> p (a c)"), n_hi[:, 0:2, :].rearrange("p a c -> p (a c)"))
            group_var_in(0, 4)
            acc_lo(4, 1, n_lo[:, 2:4, :].rearrange("p a c -> p (a c)"), n_hi[:, 2:4, :].rearrange("p a c -> p (a c)"))
            dve.wait_ge(side_drained, 1)
            for c in range(CT):
                normalise(c)
                split_xn(0, c)
                add_r(0, c)
            split_r(0)

            def image(b, more):
                job = SETUP_JOBS + JOBS * b
                sjob = SETUP_SIDE + SIDES * b
                his = SETUP_HI + HIS * b

                def turned_lo(i, h):
                    dve.wait_ge(side_hi_ready, 2 * NT * b + 2 * i + h + 1)
                    at = (slice(None), slice(h * JT, (h + 1) * JT), slice(i * P, (i + 1) * P))
                    dve.tensor_tensor(at_lo[at], side[:, h, :].rearrange("p (t n) -> p t n", t=JT),
                                      at_hi[at].bitcast(f32), ALU.subtract).then_inc(side_drained, 1)

                def scores(i):
                    gate(acc_filled, job + S0 + i + 1)
                    dve.tensor_tensor_reduce(out=prob[i % PB], in0=acc[i % 2][:, :], in1=r_row, scale=-SCALE,
                                             scalar=3.0e38, op0=ALU.add, op1=ALU.min,
                                             accum_out=neg_max[:, i:i + 1]).then_inc(acc_drained, 1)

                def normalise_rows(i):
                    dve.wait_ge(exp_ready, NT * b + i + 1)
                    dve.reciprocal(row_inv[:, i:i + 1], row_sum[:, i:i + 1]).then_inc(inv_ready, 1)
                    dve.wait_ge(inv_ready, NT * b + i + 1)
                    dve.tensor_scalar(prob[i % PB], prob[i % PB], row_inv[:, i:i + 1], None,
                                      ALU.mult).then_inc(prob_ready, 1)

                def output(c):
                    dve.wait_ge(acc_filled, job + V0 + c + 1)
                    dve.wait_ge(res_loaded[c % 2], 16 * (CT // 2) * b + 16 * (c // 2 + 1))
                    dve.scalar_tensor_tensor(x_res[:, c % 2, :], acc[c % 2][:, :], g_col[:, c:c + 1], x_res[:, c % 2, :],
                                             ALU.add, ALU.add).then_inc(acc_drained, 1)

                for c in range(CT):
                    dve.wait_ge(acc_hi_ready, his + c + 1)
                    dve.scalar_tensor_tensor(y_lo[:, c, :], acc[c % 2][:, :], u_col[:, c:c + 1],
                                             y_hi[:, c, :].bitcast(f32), ALU.add, ALU.subtract).then_inc(acc_drained, 1)
                    if c == 1:
                        dve.wait_ge(side_filled, sjob + 1)
                        dve.tensor_scalar(r_row, side[:, :, :].rearrange("p h n -> p (h n)"), r_const, None,
                                          ALU.add).then_inc(side_drained, 1)
                dve.wait_ge(side_drained, sjob + 1)
                for n in range(NT + NT // 2):
                    if 2 <= n < NT + 2:
                        turned_lo(n - 2, 0)
                    if n < NT:
                        scores(n)
                    if 2 <= n < NT + 2:
                        turned_lo(n - 2, 1)
                    if n < NT:
                        normalise_rows(n)
                    else:
                        z = n - NT
                        cols = slice(2 * z * C, (2 * z + 2) * C)
                        acc_lo(his + CT + z + 1, z % 2, yz_lo[:, cols], yz_hi[:, cols])
                        if more and z >= 2:
                            for c in range(2 * z - 4, 2 * z - 2):
                                channel_stats(b + 1, c)
                if more:
                    group_mean_in(b + 1, sjob + SIDE_STAT + 1)
                output(0)
                if more:
                    group_var_in(b + 1, sjob + SIDE_STAT + 2)
                    normalise(0)
                    normalise(1)
                    for c in range(CT):
                        split_xn(b + 1, c)
                        add_r(b + 1, c)
                        if c + 2 < CT:
                            normalise(c + 2)
                        if c == 1:
                            output(1)
                else:
                    output(1)
                output(2)
                output(3)
                if more:
                    split_r(b + 1)

            images(dve, image)


def kernel(x, L0_conv_gamma, L0_conv_beta, L0_conv_wq, L0_conv_bq, L0_conv_wk, L0_conv_bk, L0_conv_wv, L0_conv_bv,
           L0_conv_wp, L0_conv_bp):
    import numpy as np
    import concourse.bacc as bacc
    from concourse.bass_utils import run_bass_kernel_spmd

    x = np.asarray(x)
    b, c, h, w = x.shape
    vectors = np.stack([np.asarray(v) for v in (L0_conv_gamma, L0_conv_beta, L0_conv_bq, L0_conv_bk, L0_conv_bv, L0_conv_bp)])
    vectors = vectors.reshape(6, c // 128, 128).transpose(2, 0, 1).reshape(128, -1)
    arrays = {
        "x": x.reshape(b, c, h * w),
        "wq": np.asarray(L0_conv_wq),
        "wk": np.asarray(L0_conv_wk),
        "wv": np.asarray(L0_conv_wv),
        "wp_t": np.asarray(L0_conv_wp).T,
        "vectors": vectors,
    }
    arrays = {name: np.ascontiguousarray(a) for name, a in arrays.items()}
    nc = bacc.Bacc("TRN2", target_bir_lowering=False, num_devices=1)
    args = [nc.dram_tensor(name, a.shape, mybir.dt.from_np(a.dtype), kind="ExternalInput").ap()
            for name, a in arrays.items()]
    out = nc.dram_tensor("out", (b, c, h * w), mybir.dt.from_np(x.dtype), kind="ExternalOutput").ap()
    groupnorm_attention(nc, *args, out)
    results = run_bass_kernel_spmd(nc, [arrays], core_ids=[0])
    return results.results[0]["out"].reshape(b, c, h, w)
```

```python
from contextlib import ExitStack

import concourse.bass as bass
from concourse import mybir


def groupnorm_attention(nc, x, wq, wk, wv, wp_t, vectors, out):
    f32 = mybir.dt.float32
    f32r = mybir.dt.float32r
    ALU = mybir.AluOpType
    ACT = mybir.ActivationFunctionType
    AX = mybir.AxisListType

    P = 128
    B, C, N = x.shape
    GROUPS = 8
    EPS = 1e-5
    CT = C // P
    NT = N // P
    H = 512
    NH = N // H
    GC = C // GROUPS
    SCALE = float(C) ** -0.5
    JT = H // P
    assert NH == 2 and C == H and P % GC == 0

    SETUP_JOBS = 4
    JOBS = CT + NT + NT // 2 + CT
    Y0, S0 = 0, CT
    Z0 = S0 + NT
    V0 = Z0 + NT // 2
    R_AFTER = 2
    assert JOBS % 2 == 0 and SETUP_JOBS % 2 == 0
    SETUP_SIDE = 3
    SIDE_T = 1
    SIDE_STAT = SIDE_T + 2 * NT
    SIDES = SIDE_STAT + 2

    ctx = ExitStack()
    with ctx:
        def sb(name, shape, dt=f32):
            return ctx.enter_context(nc.sbuf_tensor(name, shape, dt))

        def sem(name):
            return ctx.enter_context(nc.semaphore(name))

        x_in = sb("x_in", [P, CT, N])
        x_res = sb("x_res", [P, 2, N])
        xn_hi, xn_lo = sb("xn_hi", [P, CT, N], f32r), sb("xn_lo", [P, CT, N], f32r)
        yz_hi, yz_lo = sb("yz_hi", [P, CT * N], f32r), sb("yz_lo", [P, CT * N], f32r)
        at_hi, at_lo = sb("at_hi", [P, NT, N], f32r), sb("at_lo", [P, NT, N], f32r)
        m_hi, m_lo = sb("m_hi", [P, CT, C], f32r), sb("m_lo", [P, CT, C], f32r)
        n_hi, n_lo = sb("n_hi", [P, CT, C], f32r), sb("n_lo", [P, CT, C], f32r)
        work = sb("work", [P, 4, N])
        r_part = sb("r_part", [P, N])
        ident = sb("ident", [P, P])
        group_mean = sb("group_mean", [P, P], f32r)
        sum_hi, sum_lo = sb("sum_hi", [P, CT], f32r), sb("sum_lo", [P, CT], f32r)
        ones_r = sb("ones_r", [P, P], f32r)
        vec = sb("vec", [P, 6, CT])
        gamma, beta, bq, bk, bv, bp = (vec[:, n, :] for n in range(6))
        w_col, u_col = sb("w_col", [P, CT]), sb("u_col", [P, CT])
        r_const = sb("r_const", [P, 1])
        g_col = sb("g_col", [P, CT])
        bqk = sb("bqk", [P, CT])
        stats = sb("stats", [P, CT, NH, 6])
        mean_var = sb("mean_var", [P, CT, 2])
        mean_g, dev, sq, sqv, var_g = (sb(n, [P, CT]) for n in ("mean_g", "dev", "sq", "sqv", "var_g"))
        half_neg, rstd, x_scale, ms, x_shift = (
            sb(n, [P, CT]) for n in ("half_neg", "rstd", "x_scale", "ms", "x_shift"))
        neg_max, row_sum, row_inv = (sb(n, [P, NT]) for n in ("neg_max", "row_sum", "row_inv"))

        y_hi, y_lo = (t[:, :].rearrange("p (c n) -> p c n", c=CT) for t in (yz_hi, yz_lo))
        z_hi, z_lo = (t[:, :].rearrange("p (t c) -> p t c", t=NT) for t in (yz_hi, yz_lo))
        PB = 3
        prob = [work[:, n, :] for n in range(PB)]
        r_row = work[:, PB, :]
        r_half = work[0:P // 2, PB - 1, :]
        ones = ones_r[:, :].bitcast(f32)
        wk_in, wq_in = (work[:, 2 * n:2 * n + 2, :].rearrange("p a (b c) -> p (a b) c", c=C) for n in range(2))
        wv_in = x_res[:, :, :].rearrange("p a (b c) -> p (a b) c", c=C)
        wp_in = x_in[:, 2:4, :].rearrange("p a (b c) -> p (a b) c", c=C)
        parts_hi, parts_lo = (
            [t[:, 2 * n:2 * n + 2, :].rearrange("p a (b c) -> p (a b) c", c=C) for n in range(4)]
            for t in (at_hi, at_lo))
        WK, WQ, WV, WP = range(4)
        wb_terms = [[wk_in[:, k, :] for k in range(CT)], [wq_in[:, k, :] for k in range(CT)],
                    [wk_in[:, 1, :], wk_in[:, 2, :], wk_in[:, 3, :], wq_in[:, 1, :]]]
        WB_STEPS = 7

        acc = [ctx.enter_context(nc.psum_tensor(f"acc{n}", [P, N], f32)) for n in range(2)]
        side = ctx.enter_context(nc.psum_tensor("side", [P, NH, H], f32))

        vec_loaded = sem("vec_loaded")
        wk_loaded, wq_loaded = ([sem(f"{w}{k}_loaded") for k in range(CT)] for w in ("wk", "wq"))
        wv_loaded, wp_loaded = sem("wv_loaded"), sem("wp_loaded")
        x_loaded = [sem(f"x_loaded{n}") for n in range(CT)]
        res_loaded = [sem(f"res_loaded{n}") for n in range(2)]
        out_stored = [sem(f"out_stored{n}") for n in range(2)]
        consts_ready = sem("consts_ready")
        ident_zeroed = sem("ident_zeroed")
        setup_ready = sem("setup_ready")
        group_mean_zeroed = sem("group_mean_zeroed")
        wb_step = sem("wb_step")
        vectors_ready = sem("vectors_ready")
        qk_hi_ready, qk_lo_ready = sem("qk_hi_ready"), sem("qk_lo_ready")
        vp_hi_ready, vp_lo_ready = sem("vp_hi_ready"), sem("vp_lo_ready")
        acc_filled, acc_hi_ready, acc_drained = sem("acc_filled"), sem("acc_hi_ready"), sem("acc_drained")
        side_filled, side_hi_ready, side_drained = sem("side_filled"), sem("side_hi_ready"), sem("side_drained")
        exp_ready, inv_ready, prob_ready = sem("exp_ready"), sem("inv_ready"), sem("prob_ready")
        stats_ready, mean_ready = sem("stats_ready"), sem("mean_ready")
        sum_hi_ready, sum_lo_ready = sem("sum_hi_ready"), sem("sum_lo_ready")
        norm_step, rstd_ready = sem("norm_step"), sem("rstd_ready")
        xn_ready, xn_hi_ready, xn_lo_ready = sem("xn_ready"), sem("xn_hi_ready"), sem("xn_lo_ready")
        x_used = sem("x_used")
        r_moved, r_halved = sem("r_moved"), sem("r_halved")
        r_hi_ready, r_lo_ready = sem("r_hi_ready"), sem("r_lo_ready")
        gates = sem("gates")
        NORM_STEPS = 6

        block = ctx.enter_context(nc.Block())

        def images(eng, image):
            with nc.Fori(0, B - 1, engines=[eng.engine], hint_back_edge=True) as b:
                image(b, True)
            image(B - 1, False)

        @block.sync
        def _(sp):
            weight = lambda w: w.rearrange("(t p) c -> p t c", p=P)
            for k in range(CT):
                sp.dma_start(wk_in[:, k, :], wk[k * P:(k + 1) * P, :]).then_inc(wk_loaded[k], 16)
                sp.dma_start(wq_in[:, k, :], wq[k * P:(k + 1) * P, :]).then_inc(wq_loaded[k], 16)
                if k == 0:
                    sp.dma_start(vec[:, :, :], vectors.rearrange("p (n c) -> p n c", n=6)).then_inc(vec_loaded, 16)

            def load_x(b, tiles=range(CT)):
                for c in tiles:
                    sp.dma_start(x_in[:, c, :], x[b, c * P:(c + 1) * P, :]).then_inc(x_loaded[c], 16)

            sp.dma_start(wv_in, weight(wv)).then_inc(wv_loaded, 16)
            sp.dma_start(wp_in, weight(wp_t)).then_inc(wp_loaded, 16)
            load_x(0, range(0, 2))
            sp.wait_ge(vp_lo_ready, 2)
            sp.wait_ge(wb_step, 2 * WB_STEPS + CT)
            load_x(0, range(2, CT))

            def load_res(b, c):
                sp.dma_start(x_res[:, c % 2, :], x[b, c * P:(c + 1) * P, :]).then_inc(res_loaded[c % 2], 16)

            def image(b, more):
                if more:
                    sp.wait_ge(x_used, CT * b + CT)
                    load_x(b + 1)
                for c in range(CT):
                    sp.wait_ge(acc_drained, SETUP_JOBS + JOBS * b + V0 + c + 1)
                    sp.dma_start(out[b, c * P:(c + 1) * P, :], x_res[:, c % 2, :]).then_inc(out_stored[c % 2], 16)
                    if c + 2 < CT:
                        sp.wait_ge(out_stored[c % 2], 16 * (CT // 2) * b + 16 * (c // 2 + 1))
                        load_res(b, c + 2)
                for c in range(2):
                    sp.wait_ge(out_stored[c], 16 * (CT // 2) * b + 16 * (CT // 2))
                    if more:
                        load_res(b + 1, c)

            for c in range(2):
                load_res(0, c)
            images(sp, image)

        @block.gpsimd
        def _(pool):
            pool.memset(ident[:, :], 0.0).then_inc(ident_zeroed, 1)
            pool.memset(ones, 1.0).then_inc(consts_ready, 1)
            pool.memset(half_neg[:, :], -0.5).then_inc(ident_zeroed, 1)
            pool.wait_ge(ident_zeroed, 1)
            pool.affine_select(out=ident[:, :], in_=ident[:, :], compare_op=ALU.not_equal, fill=1.0,
                               base=0, pattern=[[-1, P]], channel_multiplier=1).then_inc(consts_ready, 1)
            pool.wait_ge(ident_zeroed, 2)

            def rsqrt(n, var_drained):
                pool.wait_ge(side_drained, var_drained)
                pool.tensor_tensor(rstd[:, :], var_g[:, :], half_neg[:, :], ALU.pow).then_inc(rstd_ready, 1)

            def times_bias(n, w, bias):
                terms = wb_terms[n]
                for k in range(CT):
                    if n < 2:
                        pool.wait_ge(qk_lo_ready, 2 * k + n + 1)
                    elif k == 0:
                        pool.wait_ge(wp_loaded, 16)
                    pool.tensor_scalar(terms[k], w[:, k, :], bias[:, k:k + 1], 0.0, ALU.mult, ALU.add).then_inc(wb_step, 1)
                pool.wait_ge(wb_step, WB_STEPS * n + 4)
                pool.tensor_tensor(terms[0], terms[0], terms[1], ALU.add).then_inc(wb_step, 1)
                pool.wait_ge(wb_step, WB_STEPS * n + 5)
                pool.tensor_tensor(terms[2], terms[2], terms[3], ALU.add).then_inc(wb_step, 1)
                pool.wait_ge(wb_step, WB_STEPS * n + 6)
                pool.tensor_tensor(terms[0], terms[0], terms[2], ALU.add).then_inc(wb_step, 1)
                pool.wait_ge(wb_step, WB_STEPS * n + 7)

            pool.wait_ge(vec_loaded, 16)
            times_bias(0, wk_in, bq)
            times_bias(1, wq_in, bk)
            times_bias(2, wp_in, bv)
            rsqrt(0, 2)
            with pool.Fori(0, B - 1) as b:
                rsqrt(b + 1, SETUP_SIDE + SIDES * b + SIDES)

        @block.tensor
        def _(pe):
            def claim(job):
                if not isinstance(job, int) or job >= 2:
                    pe.wait_ge(acc_drained, job - 1)

            def passes(k_hi, k_lo, streams):
                return ([(k_hi, s, 0) for s in range(streams)] + [(k_hi, s, 1) for s in range(streams)]
                        + [(k_lo, s, 0) for s in range(streams)])

            def rows_job(job, slot, l_hi, l_lo, r_hi, r_lo, before=None, between=None):
                claim(job)
                K = len(l_hi)
                for k in range(K):
                    if before is not None:
                        before(k)
                    for n, (l, h, part) in enumerate(passes(l_hi[k], l_lo[k], NH)):
                        r = (r_hi, r_lo)[part][k]
                        last = pe.matmul(acc[slot][:, h * H:(h + 1) * H], l, r[:, h * H:(h + 1) * H],
                                         start=(k == 0 and n < NH), stop=(k == K - 1 and n >= 2 * NH))
                    if k == K - 1:
                        last.then_inc(acc_filled, 1)
                    if between is not None:
                        between(k)

            def tiles_job(job, slot, tiles, l_hi, l_lo, r_hi, r_lo, before=None, between=None):
                claim(job)
                for n, t in enumerate(tiles):
                    for k in range(CT):
                        if before is not None and n == 0:
                            before(k)
                        cols = slice(t * P, (t + 1) * P)
                        for m, (l, _, part) in enumerate(passes(l_hi[:, k, cols], l_lo[:, k, cols], 1)):
                            last = pe.matmul(acc[slot][:, n * H:(n + 1) * H], l, (r_hi, r_lo)[part][:, k, :],
                                             start=(k == 0 and m == 0), stop=(k == CT - 1 and m == 2))
                    if n == len(tiles) - 1:
                        last.then_inc(acc_filled, 1)
                    if between is not None:
                        between(n)

            def group_sum(n, job, bank):
                pe.wait_ge(sum_lo_ready, n)
                if not isinstance(job, int) or job >= SETUP_SIDE:
                    pe.wait_ge(side_drained, job - 1)
                for part in (sum_hi, sum_lo):
                    last = pe.matmul(side[:, bank, 0:CT], group_mean[:, :], part[:, :],
                                     start=(part is sum_hi), stop=(part is sum_lo))
                last.then_inc(side_filled, 1)

            def group_sum_mean(nb, job, bank=0):
                group_sum(2 * nb + 1, job, bank)

            def group_sum_var(nb, job, bank=1):
                group_sum(2 * nb + 2, job, bank)

            def sum_part(to, n):
                pe.wait_ge(wb_step, WB_STEPS * (n + 1))
                for c in range(CT):
                    last = pe.matmul(to[:, c:c + 1], wb_terms[n][0][:, c * P:(c + 1) * P], ones[:, 0:1],
                                     start=True, stop=True)
                return last

            def qk_ready(k):
                pe.wait_ge(qk_lo_ready, 2 * k + 2)
            for n in range(2):
                tiles_job(n, n % 2, (2 * n, 2 * n + 1), parts_hi[WK], parts_lo[WK], parts_hi[WQ], parts_lo[WQ],
                          before=qk_ready if n == 0 else None)
            pe.wait_ge(vp_lo_ready, 2)
            for n in range(2):
                tiles_job(2 + n, n, (2 * n, 2 * n + 1), parts_hi[WV], parts_lo[WV], parts_hi[WP], parts_lo[WP])
            pe.wait_ge(setup_ready, P // GC + 1)
            pe.wait_ge(consts_ready, 2)
            group_sum_mean(0, 0, bank=1)
            sum_part(side[:, 0, 0:CT], 0)
            sum_part(side[:, 0, CT:2 * CT], 1)
            pe.wait_ge(side_drained, 1)
            group_sum_var(0, 1)
            sum_part(side[:, 0, 2 * CT:3 * CT], 2)
            pe.matmul(side[:, 0, 3 * CT:4 * CT], ones, bqk[:, :], start=True, stop=True).then_inc(side_filled, 1)

            def image(b, more):
                job = SETUP_JOBS + JOBS * b
                sjob = SETUP_SIDE + SIDES * b

                def transposes(i, h):
                    n = SIDE_T + 2 * i + h
                    if h == 0:
                        pe.wait_ge(prob_ready, NT * b + i + 1)
                    pe.wait_ge(side_drained, sjob + (1 if i == 0 else n - 1))
                    for t in range(JT):
                        j = h * JT + t
                        last = pe.transpose(side[:, h, t * P:(t + 1) * P], prob[i % PB][:, j * P:(j + 1) * P], ident[:, :])
                    last.then_inc(side_filled, 1)

                for c in range(CT):
                    cols = slice(c * P, (c + 1) * P)

                    def chunk_ready(k):
                        pe.wait_ge(xn_lo_ready, CT * b + k + 1)
                    rows_job(job + Y0 + c, c % 2, [m_hi[:, k, cols] for k in range(CT)],
                             [m_lo[:, k, cols] for k in range(CT)],
                             [xn_hi[:, k, :] for k in range(CT)], [xn_lo[:, k, :] for k in range(CT)],
                             before=chunk_ready if c == 0 else None)
                    if c == R_AFTER:
                        pe.wait_ge(r_lo_ready, b + 1)
                        pe.wait_ge(side_drained, sjob)
                        for h in range(NH):
                            last = pe.matmul(side[:, h, :], ones_r[:, :], at_hi[:, 0, h * H:(h + 1) * H],
                                             start=True, stop=True)
                        last.then_inc(side_filled, 1)

                for i in range(NT):
                    cols = slice(i * P, (i + 1) * P)

                    def y_ready(k):
                        pe.wait_ge(acc_drained, job + Y0 + k + 1)

                    def turn(k):
                        if i >= 2 and k % 2 == 1:
                            transposes(i - 2, k // 2)
                    rows_job(job + S0 + i, i % 2, [xn_hi[:, k, cols] for k in range(CT)],
                             [xn_lo[:, k, cols] for k in range(CT)],
                             [y_hi[:, k, :] for k in range(CT)], [y_lo[:, k, :] for k in range(CT)],
                             before=y_ready if i == 0 else None, between=turn)

                for z in range(NT // 2):
                    def turn(n):
                        if z < 2:
                            transposes(NT - 2 + z, n)
                    tiles_job(job + Z0 + z, z % 2, (2 * z, 2 * z + 1), xn_hi, xn_lo, n_hi, n_lo, between=turn)

                for c in range(CT):
                    cols = slice(c * P, (c + 1) * P)

                    def z_ready(k):
                        if k == 0:
                            pe.wait_ge(side_drained, sjob + SIDE_STAT)
                        if k % 2 == 0:
                            pe.wait_ge(acc_drained, job + Z0 + k // 2 + 1)

                    def sums(k):
                        if more and k == 5 and c == 0:
                            group_sum_mean(b + 1, sjob + SIDE_STAT)
                        if more and k == 5 and c == 1:
                            group_sum_var(b + 1, sjob + SIDE_STAT + 1)
                    rows_job(job + V0 + c, c % 2, [z_hi[:, k, cols] for k in range(NT)],
                             [z_lo[:, k, cols] for k in range(NT)],
                             [at_hi[:, k, :] for k in range(NT)], [at_lo[:, k, :] for k in range(NT)],
                             before=z_ready if c == 0 else None, between=sums)

            images(pe, image)

        @block.scalar
        def _(act):
            def acc_hi(job, slot, dst, bias=None):
                act.wait_ge(acc_filled, job + 1)
                if bias is None:
                    ins = act.activation(dst, acc[slot][:, :], ACT.Copy)
                else:
                    ins = act.activation(dst, acc[slot][:, :], ACT.Identity, bias=bias)
                ins.then_inc(acc_hi_ready, 1)

            def normalise(nb):
                for c in range(CT):
                    act.wait_ge(xn_ready, CT * nb + c + 1)
                    if c == 0 and not (isinstance(nb, int) and nb == 0):
                        act.wait_ge(acc_filled, SETUP_JOBS + JOBS * nb - JOBS + V0)
                    act.activation(xn_hi[:, c, :], x_in[:, c, :], ACT.Copy).then_inc(xn_hi_ready, 1)

            def split_r(nb):
                act.wait_ge(x_used, CT * nb + CT)
                act.activation(r_half[:, :], r_part[P // 2:P, :], ACT.Copy).then_inc(r_moved, 1)
                act.wait_ge(r_halved, nb + 1)
                act.wait_ge(acc_filled, SETUP_JOBS + JOBS * nb)
                act.activation(at_hi[0:P // 2, 0, :], r_part[0:P // 2, :], ACT.Copy).then_inc(r_hi_ready, 1)

            for k in range(CT):
                act.wait_ge(wk_loaded[k], 16)
                act.activation(parts_hi[WK][:, k, :], wk_in[:, k, :], ACT.Copy).then_inc(qk_hi_ready, 1)
                act.wait_ge(wq_loaded[k], 16)
                act.activation(parts_hi[WQ][:, k, :], wq_in[:, k, :], ACT.Copy).then_inc(qk_hi_ready, 1)
            act.wait_ge(wv_loaded, 16)
            act.activation(parts_hi[WV], wv_in, ACT.Copy).then_inc(vp_hi_ready, 1)
            acc_hi(0, 0, m_hi[:, 0:2, :].rearrange("p a c -> p (a c)"))
            act.wait_ge(wp_loaded, 16)
            act.activation(parts_hi[WP], wp_in, ACT.Copy).then_inc(vp_hi_ready, 1)
            acc_hi(1, 1, m_hi[:, 2:4, :].rearrange("p a c -> p (a c)"))
            acc_hi(2, 0, n_hi[:, 0:2, :].rearrange("p a c -> p (a c)"))
            acc_hi(3, 1, n_hi[:, 2:4, :].rearrange("p a c -> p (a c)"))
            normalise(0)
            act.wait_ge(vectors_ready, 3)

            def image(b, more):
                job = SETUP_JOBS + JOBS * b
                sjob = SETUP_SIDE + SIDES * b

                def turned_hi(i, h):
                    act.wait_ge(side_filled, sjob + SIDE_T + 2 * i + h + 1)
                    act.activation(at_hi[:, h * JT:(h + 1) * JT, i * P:(i + 1) * P],
                                   side[:, h, :].rearrange("p (t n) -> p t n", t=JT), ACT.Copy).then_inc(side_hi_ready, 1)

                for c in range(CT):
                    acc_hi(job + Y0 + c, c % 2, y_hi[:, c, :], bias=u_col[:, c:c + 1])
                    if c == 0:
                        split_r(b)
                for n in range(NT + NT // 2):
                    if 2 <= n < NT + 2:
                        turned_hi(n - 2, 0)
                        turned_hi(n - 2, 1)
                    if n < NT:
                        act.wait_ge(acc_drained, job + S0 + n + 1)
                        act.activation(prob[n % PB], prob[n % PB], ACT.Exp, bias=neg_max[:, n:n + 1], scale=-1.0,
                                       accum_out=row_sum[:, n:n + 1]).then_inc(exp_ready, 1)
                    else:
                        z = n - NT
                        acc_hi(job + Z0 + z, z % 2, yz_hi[:, 2 * z * C:(2 * z + 2) * C])
                if more:
                    normalise(b + 1)

            images(act, image)

        @block.vector
        def _(dve):
            def low(lo, src, hi):
                return dve.tensor_tensor(lo, src, hi.bitcast(f32), ALU.subtract)

            SETUP_HI, HIS = SETUP_JOBS, CT + NT // 2

            def acc_lo(his, slot, lo, hi):
                dve.wait_ge(acc_hi_ready, his)
                dve.tensor_tensor(lo, acc[slot][:, :], hi.bitcast(f32), ALU.subtract).then_inc(acc_drained, 1)

            def gate(semaphore, value):
                dve.wait_ge(semaphore, value)
                dve.sem_inc(gates, 1)

            def setup_lo(n):
                lo, hi = ((m_lo, m_hi), (n_lo, n_hi))[n // 2]
                rows = slice(2 * (n % 2), 2 * (n % 2) + 2)
                acc_lo(n + 1, n % 2, lo[:, rows, :].rearrange("p a c -> p (a c)"), hi[:, rows, :].rearrange("p a c -> p (a c)"))

            def channel_stats(nb, c):
                dve.wait_ge(x_loaded[c], 16 * nb + 16)
                for h in range(NH):
                    dve.bn_stats(stats[:, c, h, :], x_in[:, c, h * H:(h + 1) * H]).then_inc(stats_ready, 1)
                gate(stats_ready, NH * (CT * nb + c + 1))
                dve.bn_aggr(mean_var[:, c, :], stats[:, c, :, :].rearrange("p h s -> p (h s)")).then_inc(mean_ready, 1)

            def split_sum(n, values):
                dve.tensor_copy(sum_hi[:, :], values).then_inc(sum_hi_ready, 1)
                dve.wait_ge(sum_hi_ready, n)
                low(sum_lo[:, :], values, sum_hi[:, :]).then_inc(sum_lo_ready, 1)

            def group_mean_in(nb, filled, bank=0):
                dve.wait_ge(side_filled, filled)
                dve.tensor_copy(mean_g[:, :], side[:, bank, 0:CT]).then_inc(norm_step, 1)
                dve.tensor_tensor(dev[:, :], mean_var[:, :, 0], side[:, bank, 0:CT], ALU.subtract).then_inc(side_drained, 1)
                dve.wait_ge(side_drained, filled)
                dve.tensor_tensor(sq[:, :], dev[:, :], dev[:, :], ALU.mult).then_inc(norm_step, 1)
                dve.wait_ge(norm_step, NORM_STEPS * nb + 2)
                dve.tensor_tensor(sqv[:, :], sq[:, :], mean_var[:, :, 1], ALU.add).then_inc(norm_step, 1)
                dve.wait_ge(norm_step, NORM_STEPS * nb + 3)
                split_sum(2 * nb + 2, sqv[:, :])

            def group_var_in(nb, filled, bank=1):
                dve.wait_ge(side_filled, filled)
                dve.tensor_scalar(var_g[:, :], side[:, bank, 0:CT], EPS, None, ALU.add).then_inc(side_drained, 1)
                dve.wait_ge(rstd_ready, nb + 1)
                dve.tensor_tensor(x_scale[:, :], rstd[:, :], gamma, ALU.mult).then_inc(norm_step, 1)
                dve.wait_ge(norm_step, NORM_STEPS * nb + 4)
                dve.tensor_tensor(ms[:, :], mean_g[:, :], x_scale[:, :], ALU.mult).then_inc(norm_step, 1)
                dve.wait_ge(norm_step, NORM_STEPS * nb + 5)
                dve.tensor_tensor(x_shift[:, :], beta, ms[:, :], ALU.subtract).then_inc(norm_step, 1)
                dve.wait_ge(norm_step, NORM_STEPS * nb + 6)

            def normalise(c):
                dve.tensor_scalar(x_in[:, c, :], x_in[:, c, :], x_scale[:, c:c + 1], x_shift[:, c:c + 1],
                                  ALU.mult, ALU.add).then_inc(xn_ready, 1)

            def split_xn(nb, c):
                dve.wait_ge(xn_hi_ready, CT * nb + c + 1)
                dve.tensor_tensor(xn_lo[:, c, :], x_in[:, c, :], xn_hi[:, c, :].bitcast(f32),
                                  ALU.subtract).then_inc(xn_lo_ready, 1)

            def add_r(nb, c):
                if c == 0:
                    dve.tensor_scalar(r_part[:, :], x_in[:, c, :], w_col[:, c:c + 1], None, ALU.mult).then_inc(x_used, 1)
                else:
                    dve.wait_ge(x_used, CT * nb + c)
                    dve.scalar_tensor_tensor(r_part[:, :], x_in[:, c, :], w_col[:, c:c + 1], r_part[:, :],
                                             ALU.mult, ALU.add).then_inc(x_used, 1)

            def halve_r(nb):
                dve.wait_ge(r_moved, nb + 1)
                dve.tensor_tensor(r_part[0:P // 2, :], r_part[0:P // 2, :], r_half[:, :], ALU.add).then_inc(r_halved, 1)

            def split_r(nb):
                dve.wait_ge(r_hi_ready, nb + 1)
                dve.tensor_tensor(at_hi[P // 2:P, 0, :], r_part[0:P // 2, :], at_hi[0:P // 2, 0, :].bitcast(f32),
                                  ALU.subtract).then_inc(r_lo_ready, 1)

            dve.memset(group_mean[:, :].bitcast(f32), 0.0).then_inc(group_mean_zeroed, 1)
            dve.wait_ge(group_mean_zeroed, 1)
            for g in range(P // GC):
                rows = slice(g * GC, (g + 1) * GC)
                dve.memset(group_mean[rows, rows].bitcast(f32), 1.0 / GC).then_inc(setup_ready, 1)
            dve.wait_ge(vec_loaded, 16)
            dve.tensor_tensor(bqk[:, :], bq, bk, ALU.mult).then_inc(setup_ready, 1)
            for k in range(CT):
                for n, (w, src) in enumerate(((WK, wk_in), (WQ, wq_in))):
                    dve.wait_ge(qk_hi_ready, 2 * k + n + 1)
                    low(parts_lo[w][:, k, :], src[:, k, :], parts_hi[w][:, k, :]).then_inc(qk_lo_ready, 1)
            dve.wait_ge(vp_hi_ready, 1)
            low(parts_lo[WV], wv_in, parts_hi[WV]).then_inc(vp_lo_ready, 1)
            setup_lo(0)
            dve.wait_ge(vp_hi_ready, 2)
            low(parts_lo[WP], wp_in, parts_hi[WP]).then_inc(vp_lo_ready, 1)
            channel_stats(0, 0)
            setup_lo(1)
            for c in range(1, CT):
                channel_stats(0, c)
            dve.wait_ge(mean_ready, CT)
            split_sum(1, mean_var[:, :, 0])
            group_mean_in(0, 1, bank=1)
            setup_lo(2)
            group_var_in(0, 2)
            normalise(0)
            normalise(1)
            setup_lo(3)
            for c in range(CT):
                split_xn(0, c)
                if c + 2 < CT:
                    normalise(c + 2)
            dve.wait_ge(side_filled, SETUP_SIDE)
            dve.tensor_copy(w_col[:, :], side[:, 0, 0:CT]).then_inc(vectors_ready, 1)
            dve.tensor_copy(u_col[:, :], side[:, 0, CT:2 * CT]).then_inc(vectors_ready, 1)
            dve.tensor_tensor(g_col[:, :], side[:, 0, 2 * CT:3 * CT], bp, ALU.add).then_inc(vectors_ready, 1)
            dve.reduce_sum(r_const[:, :], side[:, 0, 3 * CT:4 * CT], AX.X).then_inc(side_drained, 1)
            dve.wait_ge(vectors_ready, 3)
            for c in range(CT):
                add_r(0, c)

            def image(b, more):
                job = SETUP_JOBS + JOBS * b
                sjob = SETUP_SIDE + SIDES * b
                his = SETUP_HI + HIS * b

                def turned_lo(i, h):
                    dve.wait_ge(side_hi_ready, 2 * NT * b + 2 * i + h + 1)
                    at = (slice(None), slice(h * JT, (h + 1) * JT), slice(i * P, (i + 1) * P))
                    dve.tensor_tensor(at_lo[at], side[:, h, :].rearrange("p (t n) -> p t n", t=JT),
                                      at_hi[at].bitcast(f32), ALU.subtract).then_inc(side_drained, 1)

                def scores(i):
                    gate(acc_filled, job + S0 + i + 1)
                    dve.tensor_tensor_reduce(out=prob[i % PB], in0=acc[i % 2][:, :], in1=r_row, scale=-SCALE,
                                             scalar=3.0e38, op0=ALU.add, op1=ALU.min,
                                             accum_out=neg_max[:, i:i + 1]).then_inc(acc_drained, 1)

                def normalise_rows(i):
                    dve.wait_ge(exp_ready, NT * b + i + 1)
                    dve.reciprocal(row_inv[:, i:i + 1], row_sum[:, i:i + 1]).then_inc(inv_ready, 1)
                    dve.wait_ge(inv_ready, NT * b + i + 1)
                    dve.tensor_scalar(prob[i % PB], prob[i % PB], row_inv[:, i:i + 1], None,
                                      ALU.mult).then_inc(prob_ready, 1)

                def output(c):
                    dve.wait_ge(acc_filled, job + V0 + c + 1)
                    dve.wait_ge(res_loaded[c % 2], 16 * (CT // 2) * b + 16 * (c // 2 + 1))
                    dve.scalar_tensor_tensor(x_res[:, c % 2, :], acc[c % 2][:, :], g_col[:, c:c + 1], x_res[:, c % 2, :],
                                             ALU.add, ALU.add).then_inc(acc_drained, 1)

                for c in range(CT):
                    dve.wait_ge(acc_hi_ready, his + c + 1)
                    dve.scalar_tensor_tensor(y_lo[:, c, :], acc[c % 2][:, :], u_col[:, c:c + 1],
                                             y_hi[:, c, :].bitcast(f32), ALU.add, ALU.subtract).then_inc(acc_drained, 1)
                    if c == 0:
                        halve_r(b)
                        split_r(b)
                    if c == R_AFTER:
                        dve.wait_ge(side_filled, sjob + 1)
                        dve.tensor_scalar(r_row, side[:, :, :].rearrange("p h n -> p (h n)"), r_const[:, :], None,
                                          ALU.add).then_inc(side_drained, 1)
                dve.wait_ge(side_drained, sjob + 1)
                for n in range(NT + NT // 2):
                    if 2 <= n < NT + 2:
                        turned_lo(n - 2, 0)
                    if n < NT:
                        scores(n)
                    if 2 <= n < NT + 2:
                        turned_lo(n - 2, 1)
                    if n < NT:
                        normalise_rows(n)
                    else:
                        z = n - NT
                        cols = slice(2 * z * C, (2 * z + 2) * C)
                        acc_lo(his + CT + z + 1, z % 2, yz_lo[:, cols], yz_hi[:, cols])
                        if more and z >= 2:
                            for c in range(2 * z - 4, 2 * z - 2):
                                channel_stats(b + 1, c)
                if more:
                    dve.wait_ge(mean_ready, CT * b + 2 * CT)
                    split_sum(2 * b + 3, mean_var[:, :, 0])
                    group_mean_in(b + 1, sjob + SIDE_STAT + 1)
                output(0)
                if more:
                    group_var_in(b + 1, sjob + SIDE_STAT + 2)
                    normalise(0)
                    normalise(1)
                    for c in range(CT):
                        split_xn(b + 1, c)
                        add_r(b + 1, c)
                        if c + 2 < CT:
                            normalise(c + 2)
                        if c == 1:
                            output(1)
                else:
                    output(1)
                output(2)
                output(3)

            images(dve, image)


def kernel(x, L0_conv_gamma, L0_conv_beta, L0_conv_wq, L0_conv_bq, L0_conv_wk, L0_conv_bk, L0_conv_wv, L0_conv_bv,
           L0_conv_wp, L0_conv_bp):
    import numpy as np
    import concourse.bacc as bacc
    from concourse.bass_utils import run_bass_kernel_spmd

    x = np.asarray(x)
    b, c, h, w = x.shape
    vectors = np.stack([np.asarray(v) for v in (L0_conv_gamma, L0_conv_beta, L0_conv_bq, L0_conv_bk, L0_conv_bv, L0_conv_bp)])
    vectors = vectors.reshape(6, c // 128, 128).transpose(2, 0, 1).reshape(128, -1)
    arrays = {
        "x": x.reshape(b, c, h * w),
        "wq": np.asarray(L0_conv_wq),
        "wk": np.asarray(L0_conv_wk),
        "wv": np.asarray(L0_conv_wv),
        "wp_t": np.asarray(L0_conv_wp).T,
        "vectors": vectors,
    }
    arrays = {name: np.ascontiguousarray(a) for name, a in arrays.items()}
    nc = bacc.Bacc("TRN2", target_bir_lowering=False, num_devices=1)
    args = [nc.dram_tensor(name, a.shape, mybir.dt.from_np(a.dtype), kind="ExternalInput").ap()
            for name, a in arrays.items()]
    out = nc.dram_tensor("out", (b, c, h * w), mybir.dt.from_np(x.dtype), kind="ExternalOutput").ap()
    groupnorm_attention(nc, *args, out)
    results = run_bass_kernel_spmd(nc, [arrays], core_ids=[0])
    return results.results[0]["out"].reshape(b, c, h, w)
```
